# Optimizing a Trainium2 kernel written in Bass

```python
import numpy as np
import jax
import jax.numpy as jnp

def _softmax(x, axis=-1):
    return jax.nn.softmax(x, axis=axis)

def _gelu(x):
    return jax.nn.gelu(x, approximate=True)

def _silu(x):
    return jax.nn.silu(x)

def _sigmoid(x):
    return jax.nn.sigmoid(x)

def _layernorm(x, axis=-1, eps=1e-05):
    m = jnp.mean(x, axis=axis, keepdims=True)
    v = jnp.var(x, axis=axis, keepdims=True)
    return (x - m) / jnp.sqrt(v + eps)

def _scatter_add(tgt, idx, src, axis=0):
    return tgt.at[idx].add(src)

def _segment_sum(src, seg, n):
    return jax.ops.segment_sum(src, seg, n)
kernel_name = 'mk_gnn_preln_d2_gnn_r64_7dc5a7'

def setup_inputs(seed: int=0):
    np.random.seed(seed)
    _w = jnp.asarray

    def _rec_inputs():
        import jax
        import jax.numpy as jnp
        _gk = jax.random.key(seed)
        x = -0.0009044 + 1 * jax.random.normal(jax.random.fold_in(_gk, 1), (100000, 32), jnp.float32)
        src = jax.random.randint(jax.random.fold_in(_gk, 2), (50000,), 0, 100000, jnp.int32)
        dst = jax.random.randint(jax.random.fold_in(_gk, 3), (50000,), 0, 100000, jnp.int32)
        _o = jnp.argsort(dst, stable=True)
        src = src[_o]
        dst = dst[_o]
        edge_attr_32 = 0.000196303 + 1.00016 * jax.random.normal(jax.random.fold_in(_gk, 12), (50000, 32), jnp.float32)
        return (x, src, dst, edge_attr_32)
    x, src, dst, edge_attr_32 = _rec_inputs()

    def _L0_gnn_setup():
        import jax, jax.numpy as jnp
        import numpy as np
        N_NODES = 50000
        N_EDGES = 12500
        X_DIM = 32
        E_DIM = 32
        HID = 64
        OUT = 32
        key = jax.random.key(seed)
        ks = jax.random.split(key, 6)
        x = jax.random.normal(ks[0], (N_NODES, X_DIM), dtype=jnp.float32)
        edge_index = jax.random.randint(ks[1], (2, N_EDGES), 0, N_NODES, dtype=jnp.int64)
        edge_attr = jax.random.normal(ks[2], (N_EDGES, E_DIM), dtype=jnp.float32)
        in_dim = 2 * X_DIM + E_DIM
        W1 = jax.random.normal(ks[3], (in_dim, HID), dtype=jnp.float32) * (1.0 / np.sqrt(in_dim))
        b1 = jnp.zeros((HID,), dtype=jnp.float32)
        W2 = jax.random.normal(ks[4], (HID, OUT), dtype=jnp.float32) * (1.0 / np.sqrt(HID))
        b2 = jnp.zeros((OUT,), dtype=jnp.float32)
        return {'x': x, 'edge_index': edge_index, 'edge_attr': edge_attr, 'W1': W1, 'b1': b1, 'W2': W2, 'b2': b2}
    _L0_gnn_all = _L0_gnn_setup()
    _L0_gnn_in = {k: v for k, v in _L0_gnn_all.items() if k in ('W1', 'b1', 'W2', 'b2')}
    del _L0_gnn_all

    def _L1_gnn_setup():
        import jax, jax.numpy as jnp
        import numpy as np
        N_NODES = 100000
        N_EDGES = 25000
        D_FEAT = 32
        key = jax.random.key(seed)
        k1, k2, k3 = jax.random.split(key, 3)
        h = jax.random.normal(k1, (N_NODES, D_FEAT), dtype=jnp.float32)
        src = jax.random.randint(k2, (N_EDGES,), 0, N_NODES, dtype=jnp.int64)
        dst = jax.random.randint(k3, (N_EDGES,), 0, N_NODES, dtype=jnp.int64)
        return {'h': h, 'src': src, 'dst': dst}
    _L1_gnn_all = _L1_gnn_setup()
    _L1_gnn_in = {k: v for k, v in _L1_gnn_all.items() if k in ()}
    del _L1_gnn_all
    return {'x': x, 'src': src, 'dst': dst, 'edge_attr_32': edge_attr_32, 'L0_gnn_W1': _L0_gnn_in['W1'], 'L0_gnn_b1': _L0_gnn_in['b1'], 'L0_gnn_W2': _L0_gnn_in['W2'], 'L0_gnn_b2': _L0_gnn_in['b2']}

def reference(x, src, dst, edge_attr_32, L0_gnn_W1, L0_gnn_b1, L0_gnn_W2, L0_gnn_b2):
    import jax
    import jax.numpy as jnp

    def _L0_gnn_ref(x, edge_index, edge_attr, W1, b1, W2, b2):
        import jax, jax.numpy as jnp
        import numpy as np
        N_NODES = 50000
        N_EDGES = 12500
        X_DIM = 32
        E_DIM = 32
        HID = 64
        OUT = 32
        num_nodes = x.shape[0]
        rol, col = (edge_index[0], edge_index[1])
        e_feat = jnp.concatenate([x[rol], x[col], edge_attr], axis=-1)
        h = jax.nn.relu(e_feat @ W1 + b1)
        v = h @ W2 + b2
        x_cand = jax.ops.segment_max(v, col, num_segments=num_nodes)
        return jnp.maximum(x_cand, x[:, -v.shape[-1]:])

    def _L1_gnn_ref(h, src, dst):
        import jax, jax.numpy as jnp
        import numpy as np
        N_NODES = 100000
        N_EDGES = 25000
        D_FEAT = 32
        n = h.shape[0]
        msg_sum = jax.ops.segment_sum(h[src], dst, num_segments=n)
        deg = jax.ops.segment_sum(jnp.ones_like(dst, dtype=h.dtype), dst, num_segments=n)
        h_N = msg_sum / jnp.maximum(deg, 1.0)[:, None]
        return h_N
    edge_index = jnp.stack([src, dst])
    h = jnp.maximum(_layernorm(x, axis=-1), 0.0)
    x = x + _L0_gnn_ref(h, edge_index, edge_attr_32, L0_gnn_W1, L0_gnn_b1, L0_gnn_W2, L0_gnn_b2)
    h = jnp.maximum(_layernorm(x, axis=-1), 0.0)
    x = x + _L1_gnn_ref(h, src, dst)
    return x

_drawn_inputs = setup_inputs


def setup_inputs(seed=0):
    import zlib

    import numpy as np

    out = dict(_drawn_inputs(seed))
    spreads = {'L0_gnn_b1': (0.0, 0.505), 'L0_gnn_b2': (0.0, 0.293)}
    factors = {}
    for name, (base, spread) in spreads.items():
        noise = np.random.default_rng([zlib.crc32(name.encode()), seed]).standard_normal(out[name].shape)
        drawn = base * np.exp(spread * noise) if base else spread * noise
        out[name] = jnp.asarray(drawn.astype(out[name].dtype))
    for name, factor in factors.items():
        out[name] = (out[name] * factor).astype(out[name].dtype)
    return out
```

```python
from contextlib import ExitStack

import concourse.bass as bass
from concourse import mybir

F32 = mybir.dt.float32
I32 = mybir.dt.int32
ALU = mybir.AluOpType
ACT = mybir.ActivationFunctionType
AX_X = mybir.AxisListType.X

P = 128
EPS = 1e-05
BIG = 3.0e38
OUTSIDE = 1 << 17
KC = 4
GE = KC * P
NR = 8
SLOTS = 2


def sweep(eng, n, step):
    step(0)
    with eng.Fori(1, n - 1) as i:
        step(i)
    step(n - 1)


def used(eng, signal, count):
    if not (isinstance(count, int) and count == 0):
        eng.wait_ge(signal, count)


def gnn_kernel(nc, x, src, dst, edge_attr, W1, b1, W2, b2, out):
    N, D = x.shape
    E = src.shape[0]
    IN, HID = W1.shape
    G = -(-E // GE)
    FULL = E // GE
    TAIL = E - FULL * GE
    GN = P * NR
    LASTP = (N - (G - 1) * GN) // NR
    ITER = G // SLOTS
    assert G % SLOTS == 0 and (G - 1) * GN + LASTP * NR == N and 0 < LASTP <= P
    assert G <= P and FULL == G - 1 and 1 < TAIL < GE and N < OUTSIDE

    masks = nc.dram_tensor("segment_masks", (2, G, GE), F32, kind="Internal").ap()

    with ExitStack() as ctx:
        def sb(name, shape, dt=F32):
            return ctx.enter_context(nc.sbuf_tensor(name, shape, dt))

        def ps(name, shape):
            return ctx.enter_context(nc.psum_tensor(name, shape, F32))

        def sem(name):
            return ctx.enter_context(nc.semaphore(name))

        def sems(name):
            return [sem(f"{name}{u}") for u in range(SLOTS)]

        ident = sb("ident", [P, P])
        w1_sb = sb("w1_sb", [IN, HID])
        w2_sb = sb("w2_sb", [HID + 1, D])
        b1_sb = sb("b1_sb", [HID, 1])
        eps_sb = sb("eps_sb", [P, 1])
        src_rows = sb("src_rows", [G, GE], I32)
        dst_rows = sb("dst_rows", [G, GE], I32)
        prev_rows = sb("prev_rows", [G, GE], I32)
        next_rows = sb("next_rows", [G, GE], I32)
        same_prev = sb("same_prev", [G, GE])
        penalty = sb("penalty", [G, GE])
        same_next = sb("same_next", [G, GE])
        src_f = sb("src_f", [G, GE])
        dst_f = sb("dst_f", [G, GE])
        last_f = sb("last_f", [G, GE])
        pair_idx = sb("pair_idx", [P, G, 2, KC], I32)
        last_idx = sb("last_idx", [P, G, KC], I32)

        pair_now = sb("pair_now", [P, SLOTS, 2, KC], I32)
        last_now = sb("last_now", [P, SLOTS, KC], I32)
        src_now = sb("src_now", [P, SLOTS, KC], I32)
        row_now = sb("row_now", [P, SLOTS, KC, D])

        xg = sb("xg", [P, SLOTS, KC, 2, D])
        cen = sb("cen", [P, SLOTS, KC, 2, D])
        sq = sb("sq", [P, SLOTS, KC, 2, D])
        st = sb("st", [P, SLOTS, 4, 2 * KC])
        feats = sb("feats", [P, SLOTS, KC, IN])
        featT = sb("featT", [IN, SLOTS, GE])
        hidT = sb("hidT", [HID + 1, SLOTS, GE])
        pen_sb = sb("pen_sb", [D, SLOTS, GE])
        maxT = sb("maxT", [D, SLOTS, GE])
        tmp = sb("tmp", [P, SLOTS, KC, D])
        x2e = sb("x2e", [P, G, KC, D])
        dx = sb("dx", [P, SLOTS, NR, D])
        dc = sb("dc", [P, SLOTS, NR, D])
        dq = sb("dq", [P, SLOTS, NR, D])
        dst_st = sb("dense_stats", [P, SLOTS, 4, NR])
        dy = sb("dy", [P, SLOTS, NR, D])
        xs = sb("xs", [P, SLOTS, KC, D])
        cen2 = sb("cen2", [P, SLOTS, KC, D])
        sq2 = sb("sq2", [P, SLOTS, KC, D])
        st2 = sb("st2", [P, SLOTS, 4, KC])
        h2 = sb("h2", [P, SLOTS, KC, D + 1])
        same_sb = sb("same_sb", [D + 1, SLOTS, GE])
        sumT = sb("sumT", [D + 1, SLOTS, GE])
        rdeg = sb("rdeg", [P, SLOTS, KC])
        mean = sb("mean", [P, SLOTS, KC, D])

        featT_ps = [ps(f"featT_ps{u}", [P, GE]) for u in range(SLOTS)]
        hidT_ps = [ps(f"hidT_ps{u}", [HID, GE]) for u in range(SLOTS)]
        msgT_ps = [ps(f"msgT_ps{u}", [D, GE]) for u in range(SLOTS)]
        edge_ps = [ps(f"edge_ps{u}", [P, KC, P]) for u in range(SLOTS)]

        padded = sem("padded")
        lists_in = sem("lists_in")
        weights_in = sem("weights_in")
        ident_zero = sem("ident_zero")
        ident_ready = sem("ident_ready")
        masks_ready = sem("masks_ready")
        masks_out = sem("masks_out")
        prep = sem("prep")
        idx_f_ready = sem("idx_f_ready")
        idxT_ready = sem("idxT_ready")
        idx_ready = sem("idx_ready")
        ones_set = sem("ones_set")
        pair_copied = sems("pair_copied")
        src_copied = sems("src_copied")
        x2_staged = sems("x2_staged")
        final_staged = sems("final_staged")
        pool_held = sem("pool_held")
        pe_held = sem("pe_held")
        dve_held = sem("dve_held")

        gathered = sems("gathered")
        attr_in = sems("attr_in")
        pen_in = sems("pen_in")
        summed = sems("summed")
        centred = sems("centred")
        squared = sems("squared")
        var_ready = sems("var_ready")
        std_ready = sems("std_ready")
        recip_ready = sems("recip_ready")
        feats_ready = sems("feats_ready")
        featT_ready = sems("featT_ready")
        featT_copied = sems("featT_copied")
        hidden_ready = sems("hidden_ready")
        hidden_copied = sems("hidden_copied")
        msg_ready = sems("msg_ready")
        scanned = sems("scanned")
        segmax_ready = sems("segmax_ready")
        cand_ready = sems("cand_ready")
        x2_ready = sems("x2_ready")
        dense_in = sems("dense_in")
        d_summed = sems("d_summed")
        d_centred = sems("d_centred")
        d_squared = sems("d_squared")
        d_var = sems("d_var")
        d_std = sems("d_std")
        d_recip = sems("d_recip")
        d_h = sems("d_h")
        d_ready = sems("d_ready")
        dense_stored = sems("dense_stored")
        x2_scattered = sems("x2_scattered")

        gathered2 = sems("gathered2")
        same_in = sems("same_in")
        summed2 = sems("summed2")
        centred2 = sems("centred2")
        squared2 = sems("squared2")
        var2 = sems("var2")
        std2 = sems("std2")
        recip2 = sems("recip2")
        h2_ready = sems("h2_ready")
        h2T_ready = sems("h2T_ready")
        scanned2 = sems("scanned2")
        sum_ready = sems("sum_ready")
        deg_ready = sems("deg_ready")
        mean_ready = sems("mean_ready")
        final_ready = sems("final_ready")
        out_scattered = sems("out_scattered")

        block = ctx.enter_context(nc.Block())

        dense_x = x[0:(G - 1) * GN, :].rearrange("(g p r) d -> g p r d", p=P, r=NR)
        dense_o = out[0:(G - 1) * GN, :].rearrange("(g p r) d -> g p r d", p=P, r=NR)
        dense_xl = x[(G - 1) * GN:N, :].rearrange("(p r) d -> p r d", r=NR)
        dense_ol = out[(G - 1) * GN:N, :].rearrange("(p r) d -> p r d", r=NR)
        attr = edge_attr[0:FULL * GE, :].rearrange("(g k p) d -> g p k d", p=P, k=KC)
        FK = TAIL // P
        RK = TAIL - FK * P

        def rows(flat):
            return flat.rearrange("(g e) -> g e", e=GE)

        @block.sync
        def _(sp):
            sp.dma_start(w1_sb[:, :], W1).then_inc(weights_in, 16)
            sp.dma_start(w2_sb[0:HID, :], W2).then_inc(weights_in, 16)
            sp.dma_start(w2_sb[HID:HID + 1, :], b2.rearrange("(a d) -> a d", a=1)).then_inc(weights_in, 16)
            sp.dma_start(b1_sb[:, :], b1.rearrange("(d a) -> d a", a=1)).then_inc(weights_in, 16)
            sp.wait_ge(padded, 4)
            sp.dma_start(src_rows[0:FULL, :], rows(src[0:FULL * GE])).then_inc(lists_in, 16)
            sp.dma_start(src_rows[FULL:G, 0:TAIL], src[FULL * GE:E].rearrange("(g e) -> g e", g=1)).then_inc(lists_in, 16)
            sp.dma_start(dst_rows[0:FULL, :], rows(dst[0:FULL * GE])).then_inc(lists_in, 16)
            sp.dma_start(dst_rows[FULL:G, 0:TAIL], dst[FULL * GE:E].rearrange("(g e) -> g e", g=1)).then_inc(lists_in, 16)
            sp.dma_start(next_rows[0:FULL, :], rows(dst[1:FULL * GE + 1])).then_inc(lists_in, 16)
            sp.dma_start(next_rows[FULL:G, 0:TAIL - 1],
                         dst[FULL * GE + 1:E].rearrange("(g e) -> g e", g=1)).then_inc(lists_in, 16)
            sp.dma_start(prev_rows[0:1, 1:GE], dst[0:GE - 1].rearrange("(g e) -> g e", g=1)).then_inc(lists_in, 16)
            sp.dma_start(prev_rows[1:FULL, :], rows(dst[GE - 1:FULL * GE - 1])).then_inc(lists_in, 16)
            sp.dma_start(prev_rows[FULL:G, 0:TAIL],
                         dst[FULL * GE - 1:E - 1].rearrange("(g e) -> g e", g=1)).then_inc(lists_in, 16)
            sp.wait_ge(masks_ready, 1)
            sp.dma_start(masks[0], penalty[:, :]).then_inc(masks_out, 16)
            sp.dma_start(masks[1], same_prev[:, :]).then_inc(masks_out, 16)
            sp.wait_ge(masks_out, 32)

            def load_group(i, u):
                g = i * SLOTS + u
                last = isinstance(g, int) and g == G - 1
                used(sp, d_ready[u], i)
                if last:
                    sp.dma_start(dx[0:LASTP, u], dense_xl).then_inc(dense_in[u], 16)
                else:
                    sp.dma_start(dx[:, u], dense_x[g]).then_inc(dense_in[u], 16)
                used(sp, scanned[u], i)
                sp.dma_start(pen_sb[:, u, :], masks[0, g].partition_broadcast(D)).then_inc(pen_in[u], 16)
                used(sp, featT_ready[u], i)
                if last:
                    sp.dma_start(feats[:, u, 0:FK, 2 * D:IN],
                                 edge_attr[FULL * GE:FULL * GE + FK * P, :].rearrange("(k p) d -> p k d", p=P)
                                 ).then_inc(attr_in[u], 16)
                    sp.dma_start(feats[0:RK, u, FK, 2 * D:IN],
                                 edge_attr[FULL * GE + FK * P:E, :]).then_inc(attr_in[u], 16)
                else:
                    sp.dma_start(feats[:, u, :, 2 * D:IN], attr[g]).then_inc(attr_in[u], 16)

            with nc.allow_non_contiguous_dma(reason="rows of 32 words"):
                sweep(sp, ITER, lambda i: [load_group(i, u) for u in range(SLOTS)])

            def load_same(i, u):
                used(sp, scanned2[u], i)
                sp.dma_start(same_sb[:, u, :], masks[1, i * SLOTS + u].partition_broadcast(D + 1)
                             ).then_inc(same_in[u], 16)

            sweep(sp, ITER, lambda i: [load_same(i, u) for u in range(SLOTS)])

        @block.gpsimd
        def _(pool):
            pool.memset(src_rows[:, :], 0).then_inc(padded, 1)
            pool.memset(dst_rows[:, :], OUTSIDE - 1).then_inc(padded, 1)
            pool.memset(next_rows[:, :], OUTSIDE - 1).then_inc(padded, 1)
            pool.memset(prev_rows[:, :], -1).then_inc(padded, 1)
            pool.memset(ident[:, :], 0.0).then_inc(ident_zero, 1)
            pool.wait_ge(ident_zero, 1)
            pool.affine_select(out=ident[:, :], in_=ident[:, :], compare_op=ALU.not_equal, fill=1.0,
                               base=0, pattern=[[-1, P]], channel_multiplier=1).then_inc(ident_ready, 1)

            def gather_pairs(i):
                for u in range(SLOTS):
                    pool.wait_ge(pair_copied[u], i + 1)
                    used(pool, x2_ready[u], i)
                    pool.sem_inc(pool_held, 1)
                    for k in range(KC):
                        for s in range(2):
                            pool.indirect_dma_start(
                                xg[:, u, k, s, :], None, x,
                                bass.IndirectOffsetOnAxis(ap=pair_now[:, u, s, k:k + 1], axis=0)
                            ).then_inc(gathered[u], 16)

            sweep(pool, ITER, gather_pairs)

            def scatter(staged, done):
                def turn(i):
                    for u in range(SLOTS):
                        pool.wait_ge(staged[u], i + 1)
                        pool.sem_inc(pool_held, 1)
                        for k in range(KC):
                            pool.indirect_dma_start(
                                out, bass.IndirectOffsetOnAxis(ap=last_now[:, u, k:k + 1], axis=0),
                                row_now[:, u, k, :], None, bounds_check=N - 1, oob_is_err=False
                            ).then_inc(done[u], 16)
                sweep(pool, ITER, turn)
                for u in range(SLOTS):
                    pool.wait_ge(done[u], 16 * KC * ITER)

            for u in range(SLOTS):
                pool.wait_ge(dense_stored[u], 16 * ITER)
            scatter(x2_staged, x2_scattered)

            def gather_src(i):
                for u in range(SLOTS):
                    pool.wait_ge(src_copied[u], i + 1)
                    used(pool, h2_ready[u], i)
                    pool.sem_inc(pool_held, 1)
                    for k in range(KC):
                        pool.indirect_dma_start(
                            xs[:, u, k, :], None, out,
                            bass.IndirectOffsetOnAxis(ap=src_now[:, u, k:k + 1], axis=0)).then_inc(gathered2[u], 16)

            sweep(pool, ITER, gather_src)
            for u in range(SLOTS):
                pool.wait_ge(gathered2[u], 16 * KC * ITER)
            scatter(final_staged, out_scattered)

        @block.vector
        def _(dve):
            dve.memset(hidT[HID:HID + 1, :, :], 1.0).then_inc(ones_set, 1)
            dve.memset(h2[:, :, :, D:D + 1], 1.0).then_inc(ones_set, 1)
            dve.memset(eps_sb[:, :], EPS).then_inc(ones_set, 1)
            dve.wait_ge(lists_in, 9 * 16)
            dve.tensor_tensor(same_prev[:, :], dst_rows[:, :], prev_rows[:, :], ALU.is_equal).then_inc(prep, 1)
            dve.tensor_tensor(same_next[:, :], dst_rows[:, :], next_rows[:, :], ALU.is_equal).then_inc(prep, 1)
            dve.tensor_copy(src_f[:, :], src_rows[:, :]).then_inc(prep, 1)
            dve.tensor_scalar(dst_f[:, :], dst_rows[:, :], float(N - 1), None, ALU.min).then_inc(prep, 1)
            dve.wait_ge(prep, 4)
            dve.tensor_scalar(penalty[:, :], same_prev[:, :], 1.0, BIG, ALU.subtract, ALU.mult).then_inc(masks_ready, 1)
            dve.scalar_tensor_tensor(last_f[:, :], same_next[:, :], float(OUTSIDE), dst_rows[:, :],
                                     ALU.mult, ALU.add).then_inc(idx_f_ready, 1)
            for n, idx in enumerate((pair_idx[:, :, 0, :], pair_idx[:, :, 1, :], last_idx[:, :, :])):
                dve.wait_ge(idxT_ready, n + 1)
                dve.tensor_copy(idx.rearrange("p g k -> p k g"),
                                edge_ps[n % 2][:, :, 0:G]).then_inc(idx_ready, 1)

            def dense(i, u, m):
                X, C, Q, Y = (t[0:m, u] for t in (dx, dc, dq, dy))
                S, V, T, R = (dst_st[0:m, u, n, :] for n in range(4))
                Sb, Rb = (t.unsqueeze(2).to_broadcast([m, NR, D]) for t in (S, R))
                dve.wait_ge(dense_in[u], 16 * (i + 1))
                dve.tensor_reduce(S, X, AX_X, ALU.add).then_inc(d_summed[u], 1)
                dve.wait_ge(d_summed[u], i + 1)
                dve.scalar_tensor_tensor(C, Sb, -1.0 / D, X, ALU.mult, ALU.add).then_inc(d_centred[u], 1)
                yield
                dve.wait_ge(d_squared[u], i + 1)
                dve.tensor_reduce(V, Q, AX_X, ALU.add).then_inc(d_var[u], 1)
                dve.wait_ge(d_std[u], i + 1)
                dve.reciprocal(R, T).then_inc(d_recip[u], 1)
                dve.wait_ge(d_recip[u], i + 1)
                used(dve, dense_stored[u], 16 * i)
                dve.scalar_tensor_tensor(Y, C, 0.0, Rb, ALU.max, ALU.mult).then_inc(d_h[u], 1)
                dve.wait_ge(d_h[u], i + 1)
                dve.tensor_tensor(Y, Y, X, ALU.add).then_inc(d_ready[u], 1)

            def layer0(i, u):
                g = i * SLOTS + u
                last = isinstance(g, int) and g == G - 1
                X, C, Q = (t[:, u].rearrange("p k s d -> p (k s) d") for t in (xg, cen, sq))
                S, V, T, R = (st[:, u, n, :] for n in range(4))
                Sb = S.unsqueeze(2).to_broadcast([P, 2 * KC, D])
                Rb = R.rearrange("p (k s) -> p k s", s=2).unsqueeze(3).to_broadcast([P, KC, 2, D])
                H = feats[:, u, :, 0:2 * D].rearrange("p k (s d) -> p k s d", s=2)
                dve.wait_ge(gathered[u], 16 * 2 * KC * (i + 1))
                dve.tensor_reduce(S, X, AX_X, ALU.add).then_inc(summed[u], 1)
                dve.wait_ge(summed[u], i + 1)
                dve.scalar_tensor_tensor(C, Sb, -1.0 / D, X, ALU.mult, ALU.add).then_inc(centred[u], 1)
                plain = dense(i, u, LASTP if last else P)
                next(plain)
                dve.wait_ge(squared[u], i + 1)
                dve.tensor_reduce(V, Q, AX_X, ALU.add).then_inc(var_ready[u], 1)
                dve.wait_ge(std_ready[u], i + 1)
                dve.reciprocal(R, T).then_inc(recip_ready[u], 1)
                dve.wait_ge(recip_ready[u], i + 1)
                for k in range(KC):
                    ins = dve.scalar_tensor_tensor(H[:, k], cen[:, u, k], 0.0, Rb[:, k], ALU.max, ALU.mult)
                ins.then_inc(feats_ready[u], 1)
                for _ in plain:
                    pass
                dve.wait_ge(msg_ready[u], i + 1)
                dve.wait_ge(pen_in[u], 16 * (i + 1))
                if u:
                    dve.wait_ge(scanned[u - 1], i + 1)
                else:
                    used(dve, scanned[SLOTS - 1], i)
                dve.tensor_tensor_scan(maxT[:, u, :], pen_sb[:, u, :], msgT_ps[u][:, :],
                                       maxT[:, (u - 1) % SLOTS, GE - 1:GE], ALU.add, ALU.max).then_inc(scanned[u], 1)
                dve.wait_ge(segmax_ready[u], i + 1)
                dve.tensor_tensor(tmp[:, u], edge_ps[u][:, :, 0:D], feats[:, u, :, D:2 * D], ALU.max
                                  ).then_inc(cand_ready[u], 1)
                dve.wait_ge(cand_ready[u], i + 1)
                dve.tensor_tensor(x2e[:, g], tmp[:, u], xg[:, u, :, 1, :], ALU.add).then_inc(x2_ready[u], 1)

            dve.memset(maxT[:, SLOTS - 1, GE - 1:GE], 0.0).then_inc(prep, 1)
            dve.memset(sumT[:, SLOTS - 1, GE - 1:GE], 0.0).then_inc(prep, 1)
            dve.wait_ge(prep, 6)
            sweep(dve, ITER, lambda i: [layer0(i, u) for u in range(SLOTS)])

            def stage(staged, done):
                def turn(i):
                    for u in range(SLOTS):
                        used(dve, done[u], 16 * KC * i)
                        dve.sem_inc(dve_held, 1)
                        dve.tensor_copy(last_now[:, u, :], last_idx[:, i * SLOTS + u, :])
                        dve.tensor_copy(row_now[:, u], x2e[:, i * SLOTS + u]).then_inc(staged[u], 1)
                sweep(dve, ITER, turn)

            for u in range(SLOTS):
                dve.wait_ge(x2_ready[u], ITER)
            stage(x2_staged, x2_scattered)

            def layer1(i, u):
                g = i * SLOTS + u
                X, C, Q = (t[:, u] for t in (xs, cen2, sq2))
                S, V, T, R = (st2[:, u, n, :] for n in range(4))
                Sb, Rb = (t.unsqueeze(2).to_broadcast([P, KC, D]) for t in (S, R))
                dve.wait_ge(gathered2[u], 16 * KC * (i + 1))
                dve.tensor_reduce(S, X, AX_X, ALU.add).then_inc(summed2[u], 1)
                dve.wait_ge(summed2[u], i + 1)
                dve.scalar_tensor_tensor(C, Sb, -1.0 / D, X, ALU.mult, ALU.add).then_inc(centred2[u], 1)
                dve.wait_ge(squared2[u], i + 1)
                dve.tensor_reduce(V, Q, AX_X, ALU.add).then_inc(var2[u], 1)
                dve.wait_ge(std2[u], i + 1)
                dve.reciprocal(R, T).then_inc(recip2[u], 1)
                dve.wait_ge(recip2[u], i + 1)
                dve.scalar_tensor_tensor(h2[:, u, :, 0:D], C, 0.0, Rb, ALU.max, ALU.mult).then_inc(h2_ready[u], 1)
                dve.wait_ge(h2T_ready[u], i + 1)
                dve.wait_ge(same_in[u], 16 * (i + 1))
                if u:
                    dve.wait_ge(scanned2[u - 1], i + 1)
                else:
                    used(dve, scanned2[SLOTS - 1], i)
                dve.tensor_tensor_scan(sumT[:, u, :], same_sb[:, u, :], featT_ps[u][0:D + 1, :],
                                       sumT[:, (u - 1) % SLOTS, GE - 1:GE], ALU.mult, ALU.add).then_inc(scanned2[u], 1)
                dve.wait_ge(sum_ready[u], i + 1)
                dve.reciprocal(rdeg[:, u, :].unsqueeze(2), edge_ps[u][:, :, D:D + 1]).then_inc(deg_ready[u], 1)
                dve.wait_ge(deg_ready[u], i + 1)
                dve.tensor_tensor(mean[:, u], edge_ps[u][:, :, 0:D],
                                  rdeg[:, u, :].unsqueeze(2).to_broadcast([P, KC, D]), ALU.mult).then_inc(mean_ready[u], 1)
                dve.wait_ge(mean_ready[u], i + 1)
                dve.tensor_tensor(x2e[:, g], x2e[:, g], mean[:, u], ALU.add).then_inc(final_ready[u], 1)

            sweep(dve, ITER, lambda i: [layer1(i, u) for u in range(SLOTS)])
            for u in range(SLOTS):
                dve.wait_ge(final_ready[u], ITER)
                dve.wait_ge(x2_scattered[u], 16 * KC * ITER)
            stage(final_staged, out_scattered)

        @block.scalar
        def _(act):
            act.wait_ge(weights_in, 64)
            act.wait_ge(ones_set, 3)

            def number_pairs(i, u):
                act.copy(pair_now[:, u], pair_idx[:, i * SLOTS + u]).then_inc(pair_copied[u], 1)

            def layer0(i, u):
                g = i * SLOTS + u
                last = isinstance(g, int) and g == G - 1
                m = LASTP if last else P
                act.wait_ge(centred[u], i + 1)
                act.activation(sq[:, u], cen[:, u], ACT.Square, scale=D ** -0.5).then_inc(squared[u], 1)
                if not (isinstance(i, int) and i == ITER - 1):
                    number_pairs(i + 1, u)
                act.wait_ge(d_centred[u], i + 1)
                act.activation(dq[0:m, u], dc[0:m, u], ACT.Square, scale=D ** -0.5).then_inc(d_squared[u], 1)
                act.wait_ge(var_ready[u], i + 1)
                act.activation(st[:, u, 2, :], st[:, u, 1, :], ACT.Sqrt, bias=eps_sb[:, 0:1]).then_inc(std_ready[u], 1)
                act.wait_ge(d_var[u], i + 1)
                act.activation(dst_st[0:m, u, 2, :], dst_st[0:m, u, 1, :], ACT.Sqrt, bias=eps_sb[0:m, 0:1]
                               ).then_inc(d_std[u], 1)
                act.wait_ge(featT_ready[u], i + 1)
                act.activation(featT[:, u, :], featT_ps[u][0:IN, :], ACT.Copy).then_inc(featT_copied[u], 1)
                act.wait_ge(hidden_ready[u], i + 1)
                act.activation(hidT[0:HID, u, :], hidT_ps[u][:, :], ACT.Relu, bias=b1_sb[:, 0:1]
                               ).then_inc(hidden_copied[u], 1)
                act.wait_ge(d_ready[u], i + 1)
                if last:
                    act.dma_start(dense_ol, dy[0:LASTP, u]).then_inc(dense_stored[u], 16)
                else:
                    act.dma_start(dense_o[g], dy[:, u]).then_inc(dense_stored[u], 16)

            act.wait_ge(idx_ready, 3)
            for u in range(SLOTS):
                number_pairs(0, u)
            sweep(act, ITER, lambda i: [layer0(i, u) for u in range(SLOTS)])

            def number_src(i, u):
                act.copy(src_now[:, u, :], pair_idx[:, i * SLOTS + u, 0, :]).then_inc(src_copied[u], 1)

            def layer1(i, u):
                act.wait_ge(centred2[u], i + 1)
                act.activation(sq2[:, u], cen2[:, u], ACT.Square, scale=D ** -0.5).then_inc(squared2[u], 1)
                if not (isinstance(i, int) and i == ITER - 1):
                    number_src(i + 1, u)
                act.wait_ge(var2[u], i + 1)
                act.activation(st2[:, u, 2, :], st2[:, u, 1, :], ACT.Sqrt, bias=eps_sb[:, 0:1]
                               ).then_inc(std2[u], 1)

            for u in range(SLOTS):
                number_src(0, u)
            sweep(act, ITER, lambda i: [layer1(i, u) for u in range(SLOTS)])

        @block.tensor
        def _(pe):
            pe.wait_ge(ident_ready, 1)
            pe.wait_ge(prep, 4)
            pe.wait_ge(idx_f_ready, 1)
            for n, rows_f in enumerate((src_f, dst_f, last_f)):
                if n >= 2:
                    pe.wait_ge(idx_ready, n - 1)
                for k in range(KC):
                    ins = pe.transpose(edge_ps[n % 2][:, k, 0:G], rows_f[:, k * P:(k + 1) * P], ident[0:G, 0:G])
                ins.then_inc(idxT_ready, 1)
            pe.wait_ge(idx_ready, 3)
            pe.wait_ge(weights_in, 64)
            pe.wait_ge(ones_set, 3)

            def layer0(i, u):
                last = isinstance(i, int) and i * SLOTS + u == G - 1
                pe.wait_ge(feats_ready[u], i + 1)
                pe.wait_ge(attr_in[u], 16 * (i + 1) + (16 if last else 0))
                pe.sem_inc(pe_held, 1)
                for k in range(KC):
                    ins = pe.transpose(featT_ps[u][0:IN, k * P:(k + 1) * P], feats[:, u, k, :], ident[:, :])
                ins.then_inc(featT_ready[u], 1)
                pe.wait_ge(featT_copied[u], i + 1)
                pe.matmul(hidT_ps[u][:, :], w1_sb[:, :], featT[:, u, :], start=True, stop=True
                          ).then_inc(hidden_ready[u], 1)
                pe.wait_ge(hidden_copied[u], i + 1)
                pe.matmul(msgT_ps[u][:, :], w2_sb[:, :], hidT[:, u, :], start=True, stop=True
                          ).then_inc(msg_ready[u], 1)
                pe.wait_ge(scanned[u], i + 1)
                used(pe, cand_ready[u], i)
                pe.sem_inc(pe_held, 1)
                for k in range(KC):
                    ins = pe.transpose(edge_ps[u][:, k, 0:D], maxT[:, u, k * P:(k + 1) * P], ident[0:D, 0:D])
                ins.then_inc(segmax_ready[u], 1)

            sweep(pe, ITER, lambda i: [layer0(i, u) for u in range(SLOTS)])
            for u in range(SLOTS):
                pe.wait_ge(cand_ready[u], ITER)

            def layer1(i, u):
                pe.wait_ge(h2_ready[u], i + 1)
                used(pe, scanned2[u], i)
                pe.sem_inc(pe_held, 1)
                for k in range(KC):
                    ins = pe.transpose(featT_ps[u][0:D + 1, k * P:(k + 1) * P], h2[:, u, k, :], ident[:, :])
                ins.then_inc(h2T_ready[u], 1)
                pe.wait_ge(scanned2[u], i + 1)
                used(pe, mean_ready[u], i)
                pe.sem_inc(pe_held, 1)
                for k in range(KC):
                    ins = pe.transpose(edge_ps[u][:, k, 0:D + 1], sumT[:, u, k * P:(k + 1) * P],
                                       ident[0:D + 1, 0:D + 1])
                ins.then_inc(sum_ready[u], 1)

            sweep(pe, ITER, lambda i: [layer1(i, u) for u in range(SLOTS)])


_INS = ['x', 'src', 'dst', 'edge_attr_32', 'L0_gnn_W1', 'L0_gnn_b1', 'L0_gnn_W2', 'L0_gnn_b2']


def kernel(**inputs):
    import numpy as np
    import concourse.bacc as bacc
    from concourse.bass_utils import run_bass_kernel_spmd

    nc = bacc.Bacc("TRN2", target_bir_lowering=False, num_devices=1)
    arrays, args = {}, []
    for name in _INS:
        a = np.ascontiguousarray(inputs[name])
        arrays[f"in_{name}"] = a
        args.append(nc.dram_tensor(f"in_{name}", a.shape, mybir.dt.from_np(a.dtype), kind="ExternalInput").ap())
    out = nc.dram_tensor("out", inputs["x"].shape, F32, kind="ExternalOutput").ap()
    gnn_kernel(nc, *args, out)
    r = run_bass_kernel_spmd(nc, [arrays], core_ids=[0])
    return r.results[0]["out"]
```

```python
from contextlib import ExitStack

import concourse.bass as bass
from concourse import mybir

F32 = mybir.dt.float32
BF16 = mybir.dt.bfloat16
I32 = mybir.dt.int32
ALU = mybir.AluOpType
ACT = mybir.ActivationFunctionType
AX_X = mybir.AxisListType.X

P = 128
EPS = 1e-05
BIG = 3.0e38
OUTSIDE = 1 << 17
RE = 512
NB = 8
BE = NB * P
TILE = 2 * P
SHIFT = 8
HALF = 4
SLOTS = 2


def first(i):
    return isinstance(i, int) and i == 0


def used(eng, signal, count):
    if not first(count):
        eng.wait_ge(signal, count)


def gnn_kernel(nc, x, src, dst, edge_attr, W1, b1, W2, b2, out):
    N, D = x.shape
    E = src.shape[0]
    IN, HID = W1.shape
    G = 2 * -(-E // BE)
    FULL = E // RE
    TAIL = E - FULL * RE
    C = G * RE // P
    CR = RE // P
    J = C // NB
    NT = -(-N // TILE)
    W = HALF - 1
    LASTP = (N - (NT - 1) * TILE) // 2
    LT = NT - 1 - (J - 1) * NB
    STEPS = 2 * J * NB
    M = STEPS // NB
    SJ = -(-STEPS // P)
    NX = (J - 1) // 4
    FK = (E - (J - 1) * BE) // P
    RK = E - (J - 1) * BE - FK * P
    TURNS = (J + 1) // 2
    JD = 28
    J0 = J - JD
    MA = -(-(J0 * NB + NT - 1) // NB)
    GT = (J + JD + 1) // 2
    NXD = JD // 2
    assert J % 2 == 1 and J == 4 * NX + 1 and G == FULL + 1 and 1 < TAIL < RE and G <= P
    assert TILE == 1 << SHIFT and N < OUTSIDE - TILE and NT <= C and J * NB >= NT and 0 < LASTP < P
    assert JD % 2 == 0 and J0 % 2 == 1 and J < MA <= M and NX < GT - 1 and NXD < TURNS - 1
    assert STEPS >= C + NT - 1 and E <= (C - 1) * P and 0 < RK < P and D == 32

    masks = nc.dram_tensor("segment_masks", (G, RE), F32, kind="Internal").ap()
    ends_dram = nc.dram_tensor("chunk_ends", (G, CR), F32, kind="Internal").ap()
    steps_dram = nc.dram_tensor("merge_steps", (2, SJ * P), I32, kind="Internal").ap()
    x2 = nc.dram_tensor("x_after_layer_0", (N, D), F32, kind="Internal").ap()
    xends = nc.dram_tensor("x_at_ends", (J + JD, P, NB, D), F32, kind="Internal").ap()

    with ExitStack() as ctx:
        def sb(name, shape, dt=F32):
            return ctx.enter_context(nc.sbuf_tensor(name, shape, dt))

        def sem(name):
            return ctx.enter_context(nc.semaphore(name))

        def sems(name, n=SLOTS):
            return [sem(f"{name}{u}") for u in range(n)]

        nodes = sb("nodes", [P, (C + W) * 2 * (D + 1)])
        edges = sb("edges", [P, C + W, D + 1])
        xn = nodes[:, 0:C * 2 * D].rearrange("p (t h d) -> p t h d", h=2, d=D)
        acc = nodes[:, :].rearrange("p (t h d) -> p t h d", h=2, d=D + 1)
        ident = sb("ident", [P, P])
        ident_bf = sb("ident_bf", [P, P], BF16)
        node_of = sb("node_of", [P, TILE], BF16)
        tile_base = sb("tile_base", [P, C])
        w1_sb = sb("w1_sb", [IN, 3 * HID])
        w2_sb = sb("w2_sb", [2 * HID, 2 * D])
        b1_sb = sb("b1_sb", [2 * HID, 1])
        b2_sb = sb("b2_sb", [P, D])
        eps_sb = sb("eps_sb", [P, 1])
        zero = sb("zero", [P, 1])
        ends_idx = sb("ends_idx", [P, C + JD * NB], I32)
        src_idx = ends_idx[:, 0:C]
        last_idx = sb("last_idx", [P, C], I32)
        dst_col = sb("dst_col", [P, C])
        SLOT_T, PREV, TILES, CHUNKS, SLOT_C, WORDS = 0, NB, NB + 4, 2 * NB + 4, 3 * NB + 4, 4 * NB + 4
        steps = sb("steps", [1, M, WORDS], I32)
        zero_bf = sb("zero_bf", [D, HALF * 2 * (D + 1)], BF16)

        flat = edges[:, :, :].rearrange("p c d -> p (c d)")

        def piece(k, dt=F32):
            v = flat[0:G, k * RE:(k + 1) * RE]
            return v if dt == F32 else v.bitcast(dt)

        src_rows, dst_rows, prev_rows, next_rows = (piece(k, I32) for k in range(4))
        same_prev, penalty, same_next, src_f, dst_f, last_f = (piece(k) for k in range(4, 10))
        o = 10 * RE
        before = flat[:, o:o + SJ * C].rearrange("p (j c) -> p j c", c=C)
        o += SJ * C
        ends_all = flat[:, o:o + C]
        o += C
        node_i = flat[:, o:o + TILE].bitcast(I32)
        o += TILE
        base_i = flat[:, o:o + C].bitcast(I32)
        o += C
        chunk_i = flat[0:G, o:o + CR].bitcast(I32)
        o += CR
        last_dst = flat[0:G, o:o + CR].bitcast(I32)
        o += CR
        last_tile = flat[0:G, o:o + CR].bitcast(I32)
        o += CR
        ends = flat[0:G, o:o + CR]
        o += CR
        step_i = flat[:, o:o + SJ].bitcast(I32)
        o += SJ
        step_f, count, a_f, b_raw, b_f = (flat[:, o + k * SJ:o + (k + 1) * SJ] for k in range(5))
        o += 5 * SJ
        ab_i = flat[:, o:o + 2 * SJ].bitcast(I32).rearrange("p (w j) -> p w j", w=2)
        o += 2 * SJ
        assert o <= C * (D + 1)
        lists_end = o
        ACT_CLEARS = o // 2

        idx_now = sb("idx_now", [P, SLOTS, NB], I32)
        xs = sb("xs", [P, SLOTS, NB, D])
        row_now = xs
        last_now = sb("last_now", [P, SLOTS, NB], I32)

        pick = sb("pick", [P, 2, HALF, 2, P])
        shared = [sb(f"shared{k}", [P, BE]) for k in range(3)]
        pick_bf = shared[2][:, :].bitcast(BF16).rearrange("p (f q h n) -> p f q h n", f=2, q=HALF, h=2)

        R2 = 2 * NB
        dc = shared[0][:, 0:R2 * D].rearrange("p (r d) -> p r d", d=D)
        dq = shared[0][:, R2 * D:2 * R2 * D].rearrange("p (r d) -> p r d", d=D)
        dy = [shared[1][:, u * R2 * D:(u + 1) * R2 * D].rearrange("p (r d) -> p r d", d=D) for u in range(2)]
        dstat = sb("dstat", [P, 4, R2])

        xb = shared[1][:, BE // 2:BE].rearrange("p (u k d) -> p u k d", u=SLOTS, d=D)
        cen = sb("cen", [P, 2, NB, D])
        sq = sb("sq", [P, 2, NB, D])
        st = sb("st", [P, 4, 2, NB])
        featT = shared[0][0:IN, :]
        hidT = shared[1][0:2 * HID, 0:BE // 2]
        pen_sb = shared[2][0:2 * D, 0:BE // 2]
        picks_flat = pick[:, :, :, :, :].rearrange("p f q h n -> p (f q h n)")
        maxT = picks_flat[0:2 * D, 0:BE // 2]
        tmp = picks_flat[:, BE:BE + NB * D].rearrange("p (k d) -> p k d", d=D)
        feats = [sb("feats", [P, NB, IN])[:, :, :],
                 picks_flat[:, BE + NB * D:BE + NB * (D + IN)].rearrange("p (k c) -> p k c", c=IN)]
        carry = sb("carry", [2 * D, 1])

        cen2, sq2 = cen[:, 0], sq[:, 0]
        st2 = st[:, :, 0, :]
        x2n = [shared[2][:, u * R2 * D:(u + 1) * R2 * D].rearrange("p (r d) -> p r d", d=D) for u in range(2)]

        banks = [ctx.enter_context(nc.psum_tensor(f"banks{k}", [P, BE], F32)) for k in range(3)]
        edge_bank = ctx.enter_context(nc.psum_tensor("edge_bank", [P, RE], F32))
        featT_ps, hidT_ps, msgT_ps = banks[0][0:IN, :], banks[1][0:2 * HID, 0:RE], banks[2][0:2 * D, 0:RE]
        pickT_ps = [banks[0][:, f * RE:(f + 1) * RE].bitcast(BF16) for f in range(2)]
        xdst_ps = [banks[1][:, f * RE:f * RE + HALF * D].rearrange("p (q d) -> p q d", d=D) for f in range(2)]
        sum_ps = [banks[2][:, f * RE:f * RE + HALF * 2 * (D + 1)].rearrange("p (q h d) -> p q h d", q=HALF, h=2)
                  for f in range(2)]
        edge_ps = edge_bank[:, 0:NB * D].rearrange("p (k h d) -> p k h d", h=2, d=D)
        idxT_ps = [edge_bank[:, 0:CR * G].rearrange("p (k g) -> p k g", k=CR),
                   banks[2][:, 0:CR * G].rearrange("p (k g) -> p k g", k=CR)]

        padded, lists_in, weights_in = sem("padded"), sem("lists_in"), sem("weights_in")
        src_in, src_f_ready = sem("src_in"), sem("src_f_ready")
        ident_zero, ident_ready, ident_bf_ready = sem("ident_zero"), sem("ident_ready"), sem("ident_bf_ready")
        iotas_ready, masks_ready, masks_out = sem("iotas_ready"), sem("masks_ready"), sem("masks_out")
        prep = sem("prep")
        dst_idx_ready, lists_used, zeroed = sem("dst_idx_ready"), sem("lists_used"), sem("zeroed")
        ends_ready, ends_out, ends_in = sem("ends_ready"), sem("ends_out"), sem("ends_in")
        steps_ready, steps_out, steps_in = sem("steps_ready"), sem("steps_out"), sem("steps_in")
        rows_f_ready, idxT_ready, idx_ready = sem("rows_f_ready"), sem("idxT_ready"), sem("idx_ready")
        x_pad, ready, table_ready = sem("x_pad"), sem("ready"), sem("table_ready")
        idx_copied, gathered, xs_stored = sems("idx_copied"), sems("gathered"), sems("xs_stored")
        x_in = sem("x_in")
        pick_ready, pickT_ready, pickT_copied, spread = (sems(n) for n in (
            "pick_ready", "pickT_ready", "pickT_copied", "spread"))
        added = sems("added")
        d_summed, d_centred, d_squared, d_var, d_std, d_recip, d_h, d_ready = (sem(n) for n in (
            "d_summed", "d_centred", "d_squared", "d_var", "d_std", "d_recip", "d_h", "d_ready"))
        dense_stored = sem("dense_stored")
        xd_in = sem("xd_in")
        xb_in, attr_in, pen_in = sems("xb_in"), sems("attr_in"), sem("pen_in")
        weights_zero = sem("weights_zero")
        summed, centred_s, centred_d, squared, var_ready, std_ready, recip_ready, feats_ready = (sem(n) for n in (
            "summed", "centred_s", "centred_d", "squared", "var_ready", "std_ready", "recip_ready", "feats_ready"))
        featT_ready, featT_copied, hidden_ready, hidden_copied, msg_ready = (sem(n) for n in (
            "featT_ready", "featT_copied", "hidden_ready", "hidden_copied", "msg_ready"))
        scanned_a, carried_b, scanned, carried, segmax_ready, biased, cand_ready = (sem(n) for n in (
            "scanned_a", "carried_b", "scanned", "carried", "segmax_ready", "biased", "cand_ready"))
        x2_staged, x2_scattered = sems("x2_staged"), sems("x2_scattered")
        acc_zero = sem("acc_zero")
        idx2_copied, gathered2 = sems("idx2_copied"), sems("gathered2")
        summed2, centred2, squared2, var2, std2, recip2, h2_ready = (sem(n) for n in (
            "summed2", "centred2", "squared2", "var2", "std2", "recip2", "h2_ready"))
        pick2_ready, sum_ready = sems("pick2_ready"), sems("sum_ready")
        added2 = sems("added2")
        x2n_in, deg_ready, rdeg_ready, mean_ready, final_ready, out_stored = (
            sems("x2n_in"), sem("deg_ready"), sem("rdeg_ready"), sem("mean_ready"), sems("final_ready"),
            sems("out_stored"))
        pool_held, pe_held, sp_held = sem("pool_held"), sem("pe_held"), sem("sp_held")

        block = ctx.enter_context(nc.Block())

        def pairs(eng, turn, turns=TURNS, wait_rest=lambda: None):
            turn(0, SLOTS)
            wait_rest()
            with eng.Fori(1, turns - 1) as i:
                turn(i, SLOTS)
            turn(turns - 1, 1)

        node_x = x[0:(J - 1) * NB * TILE, :].rearrange("(j t p h) d -> j p t h d", t=NB, p=P, h=2)
        node_2 = x2[0:(J - 1) * NB * TILE, :].rearrange("(j t p h) d -> j p t h d", t=NB, p=P, h=2)
        node_o = out[0:(J - 1) * NB * TILE, :].rearrange("(j t p h) d -> j p t h d", t=NB, p=P, h=2)
        n0, n1 = (J - 1) * NB * TILE, (NT - 1) * TILE
        attr = edge_attr[0:(J - 1) * BE, :].rearrange("(j k p) d -> j p k d", p=P, k=NB)

        def copy_nodes(eng, dram, dram4, tiles, j, done, load):
            def move(s, d):
                (eng.dma_start(s, d) if load else eng.dma_start(d, s)).then_inc(done, 16)
            if isinstance(j, int) and j == J - 1:
                move(tiles[:, 0:LT], dram[n0:n1, :].rearrange("(t p h) d -> p t h d", p=P, h=2))
                move(tiles[0:LASTP, LT], dram[n1:N, :].rearrange("(p h) d -> p h d", h=2))
            else:
                move(tiles, dram4[j])

        def rows(v):
            return v.rearrange("(g e) -> g e", e=RE)

        def one(v):
            return v.rearrange("(g e) -> g e", g=1)

        def step_words(eng, i, at, n, top=C - 1):
            row = steps[0:1, :, :].rearrange("a m w -> a (m w)")
            row = row[:, i * WORDS + at:i * WORDS + at + n] if isinstance(i, int) else row[:, bass.ds(i * WORDS + at, n)]
            _, v = nc.values_load_multi_w_load_instructions(
                row, engines=(eng.engine,), min_val=0, max_val=top,
                skip_runtime_bounds_check_because="the table was clamped to these bounds")
            return v

        @block.sync
        def _(sp):
            sp.wait_ge(padded, 4)
            sp.dma_start(src_rows[0:FULL, :], rows(src[0:FULL * RE])).then_inc(src_in, 16)
            sp.dma_start(src_rows[FULL:G, 0:TAIL], one(src[FULL * RE:E])).then_inc(src_in, 16)
            sp.dma_start(dst_rows[0:FULL, :], rows(dst[0:FULL * RE])).then_inc(lists_in, 16)
            sp.dma_start(dst_rows[FULL:G, 0:TAIL], one(dst[FULL * RE:E])).then_inc(lists_in, 16)
            sp.dma_start(next_rows[0:FULL, :], rows(dst[1:FULL * RE + 1])).then_inc(lists_in, 16)
            sp.dma_start(next_rows[FULL:G, 0:TAIL - 1], one(dst[FULL * RE + 1:E])).then_inc(lists_in, 16)

            def load_x(j):
                used(sp, x_in, 16 * j)
                if isinstance(j, int) and j == J - 1:
                    sp.wait_ge(x_pad, 1)
                sp.sem_inc(sp_held, 1)
                copy_nodes(sp, x, node_x, xn[:, J * NB - NB:J * NB] if isinstance(j, int) and j == J - 1
                           else xn[:, bass.ds(j * NB, NB)], j, x_in, True)

            def store_ends(i, u):
                sp.wait_ge(gathered[u], 16 * NB * (i + 1))
                sp.sem_inc(sp_held, 1)
                sp.dma_start(xends[i * SLOTS + u], xs[:, u]).then_inc(xs_stored[u], 16)

            def early(i):
                for u in range(SLOTS):
                    load_x(4 * i + 2 * u)
                    load_x(4 * i + 2 * u + 1)
                    store_ends(i, u)

            early(0)
            with sp.Fori(1, NX) as i:
                early(i)
            load_x(J - 1)
            with sp.Fori(NX, GT - 2) as i:
                for u in range(SLOTS):
                    store_ends(i, u)

            sp.wait_ge(masks_out, 16)
            sp.wait_ge(spread[0], MA)
            sp.wait_ge(spread[1], MA)
            sp.wait_ge(added[1], MA + 1)

            def load_edges(i, u):
                j = i * SLOTS + u
                if not first(i):
                    sp.wait_ge(centred_s, j - 1)
                sp.sem_inc(sp_held, 1)
                sp.dma_start(xb[:, u], xends[j]).then_inc(xb_in[u], 16)
                if not first(i):
                    sp.wait_ge(featT_ready, j - 1)
                sp.sem_inc(sp_held, 1)
                if isinstance(j, int) and j == J - 1:
                    sp.dma_start(feats[u][:, 0:FK, 2 * D:IN],
                                 edge_attr[j * BE:j * BE + FK * P, :].rearrange("(k p) d -> p k d", p=P)
                                 ).then_inc(attr_in[u], 16)
                    sp.dma_start(feats[u][0:RK, FK, 2 * D:IN], edge_attr[j * BE + FK * P:E, :]).then_inc(attr_in[u], 16)
                else:
                    sp.dma_start(feats[u][:, :, 2 * D:IN], attr[j]).then_inc(attr_in[u], 16)
                if not first(i):
                    load_penalties(j - SLOTS)

            def load_penalties(b):
                used(sp, scanned, b)
                sp.sem_inc(sp_held, 1)
                for h in range(2):
                    sp.dma_start(pen_sb[h * D:(h + 1) * D, :], masks[2 * b + h].partition_broadcast(D)
                                 ).then_inc(pen_in, 16)

            def load_xdst(n):
                used(sp, xd_in, 16 * n)
                sp.sem_inc(sp_held, 1)
                sp.dma_start(edges[:, (J0 + n) * NB:(J0 + n + 1) * NB, 0:D] if isinstance(n, int)
                             else edges[:, bass.ds((n + J0) * NB, NB), 0:D], xends[n + J]).then_inc(xd_in, 16)

            def load_turn(i):
                for u in range(SLOTS):
                    load_edges(i, u)
                    load_xdst(i * SLOTS + u)

            load_edges(0, 0)
            load_edges(0, 1)
            store_ends(GT - 2, 0)
            store_ends(GT - 2, 1)
            load_edges(1, 0)
            store_ends(GT - 1, 0)
            load_edges(1, 1)
            sp.wait_ge(xs_stored[0], 16 * GT)
            sp.wait_ge(xs_stored[1], 16 * (GT - 1))
            for n in range(2 * SLOTS):
                load_xdst(n)
            with sp.Fori(2, NXD) as i:
                load_turn(i)
            with sp.Fori(NXD, TURNS - 1) as i:
                for u in range(SLOTS):
                    load_edges(i, u)
            load_edges(TURNS - 1, 0)
            load_penalties(J - 2)
            load_penalties(J - 1)

            sp.wait_ge(x2_scattered[0], 16 * NB * TURNS)
            sp.wait_ge(x2_scattered[1], 16 * NB * (TURNS - 1))
            sp.wait_ge(scanned, J)

            def load_x2(i, n):
                for u in range(n):
                    used(sp, final_ready[u], i)
                    sp.sem_inc(sp_held, 1)
                    copy_nodes(sp, x2, node_2, x2n[u].rearrange("p (t h) d -> p t h d", h=2), i * SLOTS + u,
                               x2n_in[u], True)

            pairs(sp, load_x2)

        @block.gpsimd
        def _(pool):
            pool.memset(src_rows, 0).then_inc(padded, 1)
            pool.memset(dst_rows, OUTSIDE - 1).then_inc(padded, 1)
            pool.memset(next_rows, OUTSIDE - 1).then_inc(padded, 1)
            pool.memset(prev_rows, -1).then_inc(padded, 1)
            pool.memset(ident[:, :], 0.0).then_inc(ident_zero, 1)
            pool.wait_ge(ident_zero, 1)
            pool.affine_select(out=ident[:, :], in_=ident[:, :], compare_op=ALU.not_equal, fill=1.0,
                               base=0, pattern=[[-1, P]], channel_multiplier=1).then_inc(ident_ready, 1)
            pool.iota(chunk_i, pattern=[[1, CR]], base=0, channel_multiplier=CR).then_inc(iotas_ready, 1)
            pool.iota(step_i, pattern=[[P, SJ]], base=0, channel_multiplier=1).then_inc(iotas_ready, 1)
            pool.iota(base_i, pattern=[[TILE, C]], base=0, channel_multiplier=0).then_inc(iotas_ready, 1)
            pool.iota(node_i.rearrange("p (h n) -> p h n", h=2), pattern=[[1, 2], [2, P]], base=0,
                      channel_multiplier=0).then_inc(iotas_ready, 1)

            def gathers(table, indices, copied, landed, free, turns, wait_rest=lambda: None):
                pool.tensor_copy(idx_now[:, 0, :], indices[:, 0:NB]).then_inc(copied[0], 1)

                def turn(i, n):
                    for u in range(n):
                        pool.wait_ge(copied[u], i + 1)
                        free(i, u)
                        pool.sem_inc(pool_held, 1)
                        for k in range(NB):
                            if k == NB - 2 and not (n == 1):
                                v = 1 - u
                                used(pool, landed[v], 16 * NB * (i + u))
                                pool.sem_inc(pool_held, 1)
                                pool.tensor_copy(idx_now[:, v, :], indices[:, bass.ds((i * SLOTS + u + 1) * NB, NB)]
                                                 if not isinstance(i, int) else
                                                 indices[:, (i * SLOTS + u + 1) * NB:(i * SLOTS + u + 2) * NB]
                                                 ).then_inc(copied[v], 1)
                            pool.indirect_dma_start(
                                xs[:, u, k, :], None, table,
                                bass.IndirectOffsetOnAxis(ap=idx_now[:, u, k:k + 1], axis=0)).then_inc(landed[u], 16)
                pairs(pool, turn, turns, wait_rest)

            pool.wait_ge(idx_ready, 1)
            gathers(x, ends_idx, idx_copied, gathered, lambda i, u: used(pool, xs_stored[u], 16 * i), GT,
                    lambda: pool.wait_ge(dst_idx_ready, 1))

            pool.wait_ge(dense_stored, 16 * (J + 1))

            def scatter(i, n):
                for u in range(n):
                    pool.wait_ge(x2_staged[u], i + 1)
                    pool.sem_inc(pool_held, 1)
                    for k in range(NB):
                        pool.indirect_dma_start(
                            x2, bass.IndirectOffsetOnAxis(ap=last_now[:, u, k:k + 1], axis=0),
                            row_now[:, u, k, :], None, bounds_check=N - 1, oob_is_err=False
                        ).then_inc(x2_scattered[u], 16)

            pairs(pool, scatter)
            pool.wait_ge(x2_scattered[0], 16 * NB * TURNS)
            pool.wait_ge(x2_scattered[1], 16 * NB * (TURNS - 1))

            def xs_used(i, u):
                if not first(i):
                    pool.wait_ge(centred2, i * SLOTS + u - 1)

            gathers(x2, src_idx, idx2_copied, gathered2, xs_used, TURNS)

        @block.vector
        def _(dve):
            chain = [0]

            def link(ins):
                chain[0] += 1
                ins.then_inc(prep, 1)
                dve.wait_ge(prep, chain[0])

            dve.memset(w1_sb[:, :], 0.0).then_inc(weights_zero, 1)
            dve.memset(w2_sb[:, :], 0.0).then_inc(weights_zero, 1)
            dve.memset(zero[:, :], 0.0)
            dve.memset(steps[0:1, 0:2, PREV:TILES], 0)
            dve.memset(zero_bf[:, :], 0.0)
            dve.memset(eps_sb[:, :], EPS).then_inc(prep, 1)
            dve.memset(xn[:, NT - 1:C], 0.0).then_inc(x_pad, 1)
            chain[0] += 1
            dve.memset(flat[:, lists_end:(C + W) * (D + 1)], 0.0).then_inc(zeroed, 1)
            dve.wait_ge(src_in, 2 * 16)
            dve.tensor_copy(src_f, src_rows).then_inc(src_f_ready, 1)
            dve.wait_ge(idxT_ready, 1)
            dve.tensor_copy(src_idx.rearrange("p (g k) -> p k g", k=CR), idxT_ps[0]).then_inc(idx_ready, 1)
            dve.wait_ge(lists_in, 7 * 16)
            dve.tensor_tensor(same_prev, dst_rows, prev_rows, ALU.is_equal).then_inc(prep, 1)
            dve.tensor_tensor(same_next, dst_rows, next_rows, ALU.is_equal).then_inc(prep, 1)
            dve.tensor_copy(dst_f, dst_rows).then_inc(prep, 1)
            chain[0] += 3
            link(dve.tensor_scalar(last_dst, dst_rows.rearrange("g (k e) -> g k e", e=P)[:, :, P - 1],
                                   float(N - 1), None, ALU.min))
            link(dve.tensor_scalar(last_tile, last_dst, SHIFT, None, ALU.arith_shift_right))
            dve.wait_ge(iotas_ready, 4)
            dve.tensor_tensor(ends, last_tile, chunk_i, ALU.add).then_inc(ends_ready, 1)
            dve.tensor_scalar(penalty, same_prev, 1.0, BIG, ALU.subtract, ALU.mult).then_inc(masks_ready, 1)
            dve.scalar_tensor_tensor(last_f, same_next, float(OUTSIDE), dst_rows,
                                     ALU.mult, ALU.add).then_inc(rows_f_ready, 1)
            dve.wait_ge(ident_ready, 1)
            dve.tensor_copy(ident_bf[:, :], ident[:, :]).then_inc(ident_bf_ready, 1)
            dve.tensor_copy(node_of[:, :], node_i)
            dve.tensor_copy(tile_base[:, :], base_i)
            link(dve.tensor_copy(step_f, step_i))
            for n, idx in ((1, dst_col), (2, last_idx)):
                dve.wait_ge(idxT_ready, n + 1)
                dve.tensor_copy(idx[:, :].rearrange("p (g k) -> p k g", k=CR), idxT_ps[n % 2]).then_inc(idx_ready, 1)
            dve.wait_ge(idx_ready, 2)
            dve.tensor_scalar(ends_idx[:, C:C + JD * NB], dst_col[:, J0 * NB:C], float(N - 1), None, ALU.min
                              ).then_inc(dst_idx_ready, 1)
            dve.wait_ge(ends_in, 16)
            link(dve.tensor_tensor(before, ends_all.unsqueeze(1).to_broadcast([P, SJ, C]),
                                   step_f.unsqueeze(2).to_broadcast([P, SJ, C]), ALU.is_lt))
            link(dve.tensor_reduce(count, before, AX_X, ALU.add))
            link(dve.tensor_scalar(a_f, count, float(C - 1), None, ALU.min))
            link(dve.tensor_tensor(b_raw, step_f, a_f, ALU.subtract))
            link(dve.tensor_scalar(b_f, b_raw, float(NT - 1), None, ALU.min))
            dve.tensor_copy(ab_i[:, 0, :], b_f).then_inc(steps_ready, 1)
            dve.tensor_copy(ab_i[:, 1, :], a_f).then_inc(steps_ready, 1)
            dve.wait_ge(idxT_ready, 3)
            dve.sem_inc(lists_used, 1)
            dve.wait_ge(masks_out, 16)
            dve.wait_ge(steps_out, 32)
            dve.wait_ge(zeroed, 2)
            link(dve.memset(flat[:, ACT_CLEARS:lists_end], 0.0))
            dve.memset(edges[:, :, D:D + 1], 1.0).then_inc(ready, 1)
            dve.wait_ge(steps_in, 32)

            def halves(at, n):
                return steps[0:1, :, at:at + n].rearrange("a m (f q) -> a m f q", q=HALF)

            for at, to, first_at, lag in ((TILES, SLOT_T, PREV, 1), (CHUNKS, SLOT_C, PREV + 2, 2)):
                for f in range(2):
                    v = halves(at, NB)[:, :, f, :]
                    dve.tensor_tensor(halves(to, NB)[:, :, f, :], v, v[:, :, 0:1].to_broadcast([1, M, HALF]),
                                      ALU.subtract)
                    dve.tensor_copy(steps[0:1, lag:M, first_at + f:first_at + f + 1], v[:, 0:M - lag, 0:1]
                                    ).then_inc(table_ready, 1)
            dve.wait_ge(table_ready, 4)
            dve.wait_ge(ready, 1)
            dve.wait_ge(idx_ready, 3)

            def step_picks(f, picks, tiles, chunks, done):
                for q in range(HALF):
                    n = f * HALF + q
                    ins = dve.tensor_scalar(picks[:, f, q].rearrange("p h n -> p (h n)"), node_of[:, :],
                                            tile_base[:, bass.ds(tiles[n], 1)], dst_col[:, bass.ds(chunks[n], 1)],
                                            ALU.add, ALU.is_equal)
                ins.then_inc(done[f], 1)

            def add(t, f, where, sums, sums_ready, target, totals):
                dve.wait_ge(sums_ready[f], t)
                dve.wait_ge(totals[1 - f], t)
                dve.tensor_tensor(target(where), target(where), sums[f], ALU.add).then_inc(totals[f], 1)

            def plain(i):
                X = (xn[:, i * NB:(i + 1) * NB] if isinstance(i, int) else xn[:, bass.ds(i * NB, NB)]
                     ).rearrange("p t h d -> p (t h) d")
                S, V, T, R = (dstat[:, n, :] for n in range(4))
                Sb, Rb = (t.unsqueeze(2).to_broadcast([P, R2, D]) for t in (S, R))

                def part(k):
                    if k == 0:
                        dve.wait_ge(x_in, 16 * (i + 1) + (16 if isinstance(i, int) and i == J - 1 else 0))
                        dve.tensor_reduce(S, X, AX_X, ALU.add).then_inc(d_summed, 1)
                    elif k == 1:
                        dve.wait_ge(d_summed, i + 1)
                        dve.scalar_tensor_tensor(dc, Sb, -1.0 / D, X, ALU.mult, ALU.add).then_inc(d_centred, 1)
                    elif k == 2:
                        dve.wait_ge(d_squared, i + 1)
                        dve.tensor_reduce(V, dq, AX_X, ALU.add).then_inc(d_var, 1)
                    else:
                        dve.wait_ge(d_std, i + 1)
                        dve.reciprocal(R, T).then_inc(d_recip, 1)
                        dve.wait_ge(d_recip, i + 1)
                        used(dve, dense_stored, 16 * i)
                        dve.scalar_tensor_tensor(dy[0], dc, 0.0, Rb, ALU.max, ALU.mult).then_inc(d_h, 1)
                        dve.wait_ge(d_h, i + 1)
                        dve.tensor_tensor(dy[0], dy[0], X, ALU.add).then_inc(d_ready, 1)
                return part

            def at_chunk(a):
                return edges[:, bass.ds(a, HALF), 0:D]

            def spread_turn(i, dense):
                v = step_words(dve, i, PREV + 2, 2 + 2 * NB)
                for f in range(2):
                    if not isinstance(i, int) or i >= 2:
                        add(i - 1, f, v[f], xdst_ps, spread, at_chunk, added)
                    used(dve, pickT_ready[f], i)
                    step_picks(f, pick_bf, v[2:2 + NB], v[2 + NB:], pick_ready)
                part = plain(i) if dense else None
                if dense:
                    part(0)
                    part(1)
                    part(2)
                    part(3)

            dve.sem_inc(added[1], 1)
            spread_turn(0, True)
            spread_turn(1, True)
            with dve.Fori(2, J - 1) as i:
                spread_turn(i, True)
            spread_turn(J - 1, True)
            with dve.Fori(J, MA) as i:
                spread_turn(i, False)
            for t in (MA - 1, MA):
                where = step_words(dve, t - 1, CHUNKS, NB)[::HALF]
                for f in range(2):
                    add(t, f, where[f], xdst_ps, spread, at_chunk, added)
            dve.wait_ge(added[1], MA + 1)
            dve.wait_ge(d_ready, J)
            dve.wait_ge(dense_stored, 16 * (J + 1))
            dve.wait_ge(weights_in, 96)
            dve.wait_ge(spread[1], MA)
            dve.memset(acc[:, C:C + W], 0.0)
            dve.memset(carry[:, :], 0.0).then_inc(carried, 1)

            def scan(b):
                dve.wait_ge(msg_ready, b + 1)
                dve.wait_ge(pen_in, 32 * (b + 1))
                dve.wait_ge(carried, b + 1)

                def half(lo, hi):
                    return dve.tensor_tensor_scan(maxT[lo:hi, :], pen_sb[lo:hi, :], msgT_ps[lo:hi, :],
                                                  carry[lo:hi, 0:1], ALU.add, ALU.max)

                half(0, D).then_inc(scanned_a, 1)
                dve.wait_ge(scanned_a, b + 1)
                dve.tensor_copy(carry[D:2 * D, :], maxT[0:D, RE - 1:RE]).then_inc(carried_b, 1)
                dve.wait_ge(carried_b, b + 1)
                half(D, 2 * D).then_inc(scanned, 1)

            def node_values(i, u):
                b = i * SLOTS + u
                dve.wait_ge(scanned, b + 1)
                dve.tensor_copy(carry[0:D, :], maxT[D:2 * D, RE - 1:RE]).then_inc(carried, 1)
                dve.wait_ge(segmax_ready, b + 1)
                dve.tensor_tensor(tmp.rearrange("p (h k) d -> p h k d", h=2), edge_ps.rearrange("p k h d -> p h k d"),
                                  b2_sb[:, :].unsqueeze(1).unsqueeze(1).to_broadcast([P, 2, CR, D]), ALU.add
                                  ).then_inc(biased, 1)
                dve.wait_ge(biased, b + 1)
                dve.tensor_tensor(tmp, tmp, feats[u][:, :, D:2 * D], ALU.max).then_inc(cand_ready, 1)
                used(dve, x2_scattered[u], 16 * NB * i)
                if first(i):
                    dve.wait_ge(xs_stored[u], 16 * (GT - u))
                dve.wait_ge(cand_ready, b + 1)
                if isinstance(b, int):
                    xd, li = edges[:, b * NB:(b + 1) * NB, 0:D], last_idx[:, b * NB:(b + 1) * NB]
                else:
                    xd, li = edges[:, bass.ds(b * NB, NB), 0:D], last_idx[:, bass.ds(b * NB, NB)]
                dve.tensor_tensor(row_now[:, u], tmp, xd, ALU.add)
                dve.tensor_copy(last_now[:, u, :], li).then_inc(x2_staged[u], 1)

            def layer0(i, u):
                j = i * SLOTS + u
                XD = edges[:, j * NB:(j + 1) * NB, 0:D] if isinstance(j, int) else edges[:, bass.ds(j * NB, NB), 0:D]
                S, V, T, R = (st[:, n] for n in range(4))
                Sb, Rb = (t.unsqueeze(3).to_broadcast([P, 2, NB, D]) for t in (S, R))
                dve.wait_ge(xb_in[u], 16 * (i + 1))
                dve.tensor_reduce(S[:, 0], xb[:, u], AX_X, ALU.add)
                dve.tensor_reduce(S[:, 1], XD, AX_X, ALU.add).then_inc(summed, 1)
                dve.wait_ge(summed, j + 1)
                dve.scalar_tensor_tensor(cen[:, 0], Sb[:, 0], -1.0 / D, xb[:, u], ALU.mult, ALU.add
                                         ).then_inc(centred_s, 1)
                dve.scalar_tensor_tensor(cen[:, 1], Sb[:, 1], -1.0 / D, XD, ALU.mult, ALU.add).then_inc(centred_d, 1)
                dve.tensor_copy((acc[:, j * NB:(j + 1) * NB] if isinstance(j, int) else acc[:, bass.ds(j * NB, NB)]
                                 ).rearrange("p t h d -> p (t h d)"),
                                zero[:, 0:1].to_broadcast([P, R2 * (D + 1)])).then_inc(acc_zero, 1)
                dve.wait_ge(squared, j + 1)
                dve.tensor_reduce(V, sq[:, :, :, :], AX_X, ALU.add).then_inc(var_ready, 1)
                if not first(i):
                    scan(j - SLOTS)
                dve.wait_ge(std_ready, j + 1)
                dve.reciprocal(R, T).then_inc(recip_ready, 1)
                if not first(i):
                    node_values(i - 1, u)
                dve.wait_ge(recip_ready, j + 1)
                for s in range(2):
                    ins = dve.scalar_tensor_tensor(feats[u][:, :, s * D:(s + 1) * D], cen[:, s], 0.0, Rb[:, s],
                                                   ALU.max, ALU.mult)
                ins.then_inc(feats_ready, 1)

            layer0(0, 0)
            layer0(0, 1)
            layer0(1, 0)
            layer0(1, 1)
            with dve.Fori(2, J0 // 2) as i:
                for u in range(SLOTS):
                    layer0(i, u)
            with dve.Fori(J0 // 2, TURNS - 1) as i:
                dve.wait_ge(xd_in, (i * 2 + 2 - J0) * 16)
                for u in range(SLOTS):
                    layer0(i, u)
            dve.wait_ge(xd_in, 16 * JD)
            layer0(TURNS - 1, 0)
            scan(J - 2)
            node_values(TURNS - 2, 1)
            scan(J - 1)
            node_values(TURNS - 1, 0)
            dve.wait_ge(acc_zero, J)

            def at_tile(b):
                return acc[:, bass.ds(b, HALF)].rearrange("p t h d -> p (t h d)")

            flat_sums = [s.rearrange("p q h d -> p (q h d)") for s in sum_ps]

            def sum_turn(i):
                v = step_words(dve, i, PREV, 4 + 2 * NB)
                for f in range(2):
                    if not first(i):
                        add(i, f, v[f], flat_sums, sum_ready, at_tile, added2)
                    step_picks(f, pick, v[4:4 + NB], v[4 + NB:], pick2_ready)

            def layer1(i, u):
                j = i * SLOTS + u
                X = xs[:, u]
                H = edges[:, j * NB:(j + 1) * NB, 0:D] if isinstance(j, int) else edges[:, bass.ds(j * NB, NB), 0:D]
                S, V, T, R = (st2[:, n, :] for n in range(4))
                Sb, Rb = (t.unsqueeze(2).to_broadcast([P, NB, D]) for t in (S, R))
                dve.wait_ge(gathered2[u], 16 * NB * (i + 1))
                dve.tensor_reduce(S, X, AX_X, ALU.add).then_inc(summed2, 1)
                dve.wait_ge(summed2, j + 1)
                dve.scalar_tensor_tensor(cen2, Sb, -1.0 / D, X, ALU.mult, ALU.add).then_inc(centred2, 1)
                dve.wait_ge(squared2, j + 1)
                dve.tensor_reduce(V, sq2, AX_X, ALU.add).then_inc(var2, 1)
                dve.wait_ge(std2, j + 1)
                dve.reciprocal(R, T).then_inc(recip2, 1)
                dve.wait_ge(recip2, j + 1)
                dve.scalar_tensor_tensor(H, cen2, 0.0, Rb, ALU.max, ALU.mult).then_inc(h2_ready, 1)
                sum_turn(j)

            dve.sem_inc(added2[1], 1)
            pairs(dve, lambda i, n: [layer1(i, u) for u in range(n)])
            sum_turn(J)

            assert M == 2 * J and (J + 1) * NB >= NB + C - 1

            def result(i, u, last):
                j = i * SLOTS + u
                A = (acc[:, j * NB:(j + 1) * NB] if isinstance(j, int) else acc[:, bass.ds(j * NB, NB)]
                     ).rearrange("p t h d -> p (t h) d")
                deg, rdeg = dstat[:, 0, :], dstat[:, 1, :]
                dve.tensor_scalar(deg.unsqueeze(2), A[:, :, D:D + 1], 1.0, None, ALU.max).then_inc(deg_ready, 1)
                dve.wait_ge(deg_ready, j + 1)
                dve.reciprocal(rdeg, deg).then_inc(rdeg_ready, 1)
                dve.wait_ge(rdeg_ready, j + 1)
                used(dve, out_stored[u], 16 * i)
                dve.tensor_tensor(dy[u], A[:, :, 0:D], rdeg.unsqueeze(2).to_broadcast([P, R2, D]), ALU.mult
                                  ).then_inc(mean_ready, 1)
                dve.wait_ge(mean_ready, j + 1)
                dve.wait_ge(x2n_in[u], 16 * (i + 1) + (16 if last else 0))
                dve.tensor_tensor(dy[u], dy[u], x2n[u], ALU.add).then_inc(final_ready[u], 1)

            def finish(i, n):
                for u in range(n):
                    if n == SLOTS:
                        sum_turn(i * SLOTS + (J + 1 + u))
                    else:
                        where = step_words(dve, M - 1, TILES, NB)[::HALF]
                        for f in range(2):
                            add(M, f, where[f], flat_sums, sum_ready, at_tile, added2)
                    dve.wait_ge(added2[1], i * SLOTS + (J + u + 2))
                    result(i, u, n == 1)

            pairs(dve, finish)

        @block.scalar
        def _(act):
            act.wait_ge(padded, 4)
            act.dma_start(prev_rows[0:1, 1:RE], one(dst[0:RE - 1])).then_inc(lists_in, 16)
            act.dma_start(prev_rows[1:FULL, :], rows(dst[RE - 1:FULL * RE - 1])).then_inc(lists_in, 16)
            act.dma_start(prev_rows[FULL:G, 0:TAIL], one(dst[FULL * RE - 1:E - 1])).then_inc(lists_in, 16)
            act.wait_ge(weights_zero, 2)
            act.dma_start(w1_sb[:, HID:2 * HID], W1).then_inc(weights_in, 16)
            for h in range(2):
                act.dma_start(w2_sb[h * HID:(h + 1) * HID, h * D:(h + 1) * D], W2).then_inc(weights_in, 16)
                act.dma_start(b1_sb[h * HID:(h + 1) * HID, :], b1.rearrange("(d a) -> d a", a=1)).then_inc(weights_in, 16)
            act.dma_start(b2_sb[:, :], b2.partition_broadcast(P)).then_inc(weights_in, 16)
            act.wait_ge(ends_ready, 1)
            act.dma_start(ends_dram, ends).then_inc(ends_out, 16)
            act.wait_ge(ends_out, 16)
            act.dma_start(ends_all, ends_dram.rearrange("g k -> (g k)").partition_broadcast(P)).then_inc(ends_in, 16)
            act.wait_ge(masks_ready, 1)
            act.dma_start(masks, penalty).then_inc(masks_out, 16)
            act.wait_ge(steps_ready, 2)
            with nc.allow_non_contiguous_dma(reason="a table of 1,792 words"):
                for w in range(2):
                    act.dma_start(steps_dram[w].rearrange("(j p) -> p j", p=P), ab_i[:, w, :]).then_inc(steps_out, 16)
            act.wait_ge(steps_out, 32)
            act.wait_ge(lists_used, 1)
            act.wait_ge(masks_out, 16)
            act.activation(flat[:, 0:ACT_CLEARS], zero[:, 0:1].to_broadcast([P, ACT_CLEARS]), ACT.Copy).then_inc(zeroed, 1)
            for w in range(2):
                at = TILES if w == 0 else CHUNKS
                act.dma_start(steps[0:1, :, at:at + NB],
                              steps_dram[w:w + 1, 0:STEPS].rearrange("a (m r) -> a m r", r=NB)).then_inc(steps_in, 16)
            act.wait_ge(weights_in, 96)

            def spread_turn(i, dense):
                if dense:
                    act.wait_ge(d_centred, i + 1)
                    act.activation(dq, dc, ACT.Square, scale=D ** -0.5).then_inc(d_squared, 1)
                    act.wait_ge(d_var, i + 1)
                    act.activation(dstat[:, 2, :], dstat[:, 1, :], ACT.Sqrt, bias=eps_sb[:, 0:1]).then_inc(d_std, 1)
                for f in range(2):
                    act.wait_ge(pickT_ready[f], i + 1)
                    used(act, spread[f], i)
                    act.activation(pick[:, f].rearrange("p q h n -> p (q h n)"), pickT_ps[f], ACT.Copy
                                   ).then_inc(pickT_copied[f], 1)
                if dense:
                    act.wait_ge(d_ready, i + 1)
                    copy_nodes(act, x2, node_2, dy[0].rearrange("p (t h) d -> p t h d", h=2), i, dense_stored, False)

            spread_turn(0, True)
            with act.Fori(1, J - 1) as i:
                spread_turn(i, True)
            spread_turn(J - 1, True)
            with act.Fori(J, MA) as i:
                spread_turn(i, False)

            def layer0(i, u):
                j = i * SLOTS + u
                act.wait_ge(centred_s, j + 1)
                act.activation(sq[:, 0], cen[:, 0], ACT.Square, scale=D ** -0.5)
                act.wait_ge(centred_d, j + 1)
                act.activation(sq[:, 1], cen[:, 1], ACT.Square, scale=D ** -0.5).then_inc(squared, 1)
                if not first(j):
                    features(j - 1)
                act.wait_ge(var_ready, j + 1)
                act.activation(st[:, 2], st[:, 1], ACT.Sqrt, bias=eps_sb[:, 0:1]).then_inc(std_ready, 1)
                if not first(j):
                    hidden(j - 1)

            def features(b):
                act.wait_ge(featT_ready, b + 1)
                act.activation(featT, featT_ps, ACT.Copy).then_inc(featT_copied, 1)

            def hidden(b):
                act.wait_ge(hidden_ready, b + 1)
                used(act, msg_ready, b)
                act.activation(hidT, hidT_ps, ACT.Relu, bias=b1_sb[:, 0:1]).then_inc(hidden_copied, 1)

            pairs(act, lambda i, n: [layer0(i, u) for u in range(n)])
            features(J - 1)
            hidden(J - 1)

            def layer1(i, u):
                j = i * SLOTS + u
                act.wait_ge(centred2, j + 1)
                act.activation(sq2, cen2, ACT.Square, scale=D ** -0.5).then_inc(squared2, 1)
                act.wait_ge(var2, j + 1)
                act.activation(st2[:, 2, :], st2[:, 1, :], ACT.Sqrt, bias=eps_sb[:, 0:1]).then_inc(std2, 1)

            pairs(act, lambda i, n: [layer1(i, u) for u in range(n)])

            def store(i, n):
                for u in range(n):
                    act.wait_ge(final_ready[u], i + 1)
                    copy_nodes(act, out, node_o, dy[u].rearrange("p (t h) d -> p t h d", h=2), i * SLOTS + u,
                               out_stored[u], False)

            pairs(act, store)
            act.wait_ge(out_stored[0], 16 * (TURNS + 1))
            act.wait_ge(out_stored[1], 16 * (TURNS - 1))

        @block.tensor
        def _(pe):
            pe.wait_ge(ident_ready, 1)
            pe.wait_ge(src_f_ready, 1)
            for n, rows_f in enumerate((src_f, dst_f, last_f)):
                if n == 1:
                    pe.wait_ge(prep, 4)
                if n == 2:
                    pe.wait_ge(rows_f_ready, 1)
                    pe.wait_ge(idx_ready, n - 1)
                for k in range(CR):
                    ins = pe.transpose(idxT_ps[n % 2][:, k, :], rows_f[:, k * P:(k + 1) * P], ident[0:G, 0:G])
                ins.then_inc(idxT_ready, 1)
            pe.wait_ge(ident_bf_ready, 1)
            pe.wait_ge(table_ready, 4)

            def transposes(i, f):
                pe.wait_ge(pick_ready[f], i + 1)
                used(pe, pickT_copied[f], i)
                pe.sem_inc(pe_held, 1)
                for q in range(HALF):
                    for h in range(2):
                        n = q * 2 + h
                        ins = pe.transpose(pickT_ps[f][:, n * P:(n + 1) * P], pick_bf[:, f, q, h, :], ident_bf[:, :])
                ins.then_inc(pickT_ready[f], 1)

            def spread_rows(t, f, tiles, slots):
                pe.wait_ge(pickT_copied[f], t + 1)
                if f:
                    pe.wait_ge(added[1], t + 1)
                else:
                    used(pe, added[0], t)
                pe.matmul(xdst_ps[f].rearrange("p q d -> p (q d)"), zero_bf[:, 0:P], zero_bf[:, 0:HALF * D],
                          start=True, stop=True)
                for q in range(HALF):
                    for h in range(2):
                        n = f * HALF + q
                        ins = pe.matmul(xdst_ps[f][:, bass.ds(slots[n], 1), :].rearrange("p q d -> p (q d)"),
                                        pick[:, f, q, h, :],
                                        xn[:, bass.ds(tiles[n], 1), h, :].rearrange("p t d -> p (t d)"),
                                        start=False, stop=True, skip_group_check=True)
                ins.then_inc(spread[f], 1)

            def spread_turn(i, dense, last=False):
                tiles = step_words(pe, i - 1, TILES, NB)
                slots = step_words(pe, i - 1, SLOT_C, NB, HALF - 1)
                if dense:
                    pe.wait_ge(d_summed, i)
                for f in range(2):
                    spread_rows(i - 1, f, tiles, slots)
                    if not last:
                        transposes(i, f)

            transposes(0, 0)
            transposes(0, 1)
            spread_turn(1, True)
            with pe.Fori(2, J + 1) as i:
                spread_turn(i, True)
            with pe.Fori(J + 1, MA) as i:
                spread_turn(i, False)
            spread_turn(MA, False, last=True)

            pe.wait_ge(weights_in, 96)

            def messages(b):
                pe.wait_ge(hidden_copied, b + 1)
                pe.matmul(msgT_ps, w2_sb[:, :], hidT, start=True, stop=True).then_inc(msg_ready, 1)

            def segmax(b):
                pe.wait_ge(scanned, b + 1)
                used(pe, cand_ready, b)
                pe.sem_inc(pe_held, 1)
                for k in range(CR):
                    ins = pe.transpose(edge_ps[:, k].rearrange("p h d -> p (h d)"), maxT[:, k * P:(k + 1) * P],
                                       ident[0:2 * D, 0:2 * D])
                ins.then_inc(segmax_ready, 1)

            def layer0(i, u):
                j = i * SLOTS + u
                pe.wait_ge(feats_ready, j + 1)
                pe.wait_ge(attr_in[u], 16 * (i + 1) + (16 if isinstance(j, int) and j == J - 1 else 0))
                used(pe, featT_copied, j)
                pe.sem_inc(pe_held, 1)
                for k in range(NB):
                    ins = pe.transpose(featT_ps[:, k * P:(k + 1) * P], feats[u][:, k, :], ident[:, :])
                ins.then_inc(featT_ready, 1)
                if not first(j):
                    messages(j - 1)
                pe.wait_ge(featT_copied, j + 1)
                pe.matmul(hidT_ps, w1_sb[:, HID:3 * HID], featT[:, 0:RE], start=True, stop=False)
                if not first(j):
                    segmax(j - 1)
                pe.matmul(hidT_ps, w1_sb[:, 0:2 * HID], featT[:, RE:BE], start=False, stop=True
                          ).then_inc(hidden_ready, 1)

            pairs(pe, lambda i, n: [layer0(i, u) for u in range(n)])
            messages(J - 1)
            segmax(J - 1)
            pe.wait_ge(cand_ready, J)

            def sum_turn(i, fresh):
                slots = step_words(pe, i, SLOT_T, NB, HALF - 1)
                chunks = step_words(pe, i, CHUNKS, NB)
                if fresh:
                    pe.wait_ge(h2_ready, i + 1)
                for f in range(2):
                    pe.wait_ge(pick2_ready[f], i + 1)
                    if f:
                        pe.wait_ge(added2[1], i + 1)
                    else:
                        used(pe, added2[0], i)
                    pe.matmul(sum_ps[f].rearrange("p q h d -> p (q h d)"), zero_bf[:, 0:P], zero_bf[:, :],
                              start=True, stop=True)
                    for q in range(HALF):
                        for h in range(2):
                            n = f * HALF + q
                            ins = pe.matmul(sum_ps[f][:, bass.ds(slots[n], 1), h, :].rearrange("p q d -> p (q d)"),
                                            pick[:, f, q, h, :],
                                            edges[:, bass.ds(chunks[f * HALF + q], 1), :].rearrange("p c d -> p (c d)"),
                                            start=False, stop=True, skip_group_check=True)
                    ins.then_inc(sum_ready[f], 1)

            sum_turn(0, True)
            with pe.Fori(1, J) as i:
                sum_turn(i, True)
            with pe.Fori(J, M) as i:
                sum_turn(i, False)


_INS = ['x', 'src', 'dst', 'edge_attr_32', 'L0_gnn_W1', 'L0_gnn_b1', 'L0_gnn_W2', 'L0_gnn_b2']


def kernel(**inputs):
    import numpy as np
    import concourse.bacc as bacc
    from concourse.bass_utils import run_bass_kernel_spmd

    nc = bacc.Bacc("TRN2", target_bir_lowering=False, num_devices=1)
    arrays, args = {}, []
    for name in _INS:
        a = np.ascontiguousarray(inputs[name])
        arrays[f"in_{name}"] = a
        args.append(nc.dram_tensor(f"in_{name}", a.shape, mybir.dt.from_np(a.dtype), kind="ExternalInput").ap())
    out = nc.dram_tensor("out", inputs["x"].shape, F32, kind="ExternalOutput").ap()
    gnn_kernel(nc, *args, out)
    r = run_bass_kernel_spmd(nc, [arrays], core_ids=[0])
    return r.results[0]["out"]
```
